# Optimizing a Trainium2 kernel written in Bass

```python
import numpy as np
import jax
import jax.numpy as jnp

def _softmax(x, axis=-1):
    return jax.nn.softmax(x, axis=axis)

def _gelu(x):
    return jax.nn.gelu(x, approximate=True)

def _silu(x):
    return jax.nn.silu(x)

def _sigmoid(x):
    return jax.nn.sigmoid(x)

def _layernorm(x, axis=-1, eps=1e-05):
    m = jnp.mean(x, axis=axis, keepdims=True)
    v = jnp.var(x, axis=axis, keepdims=True)
    return (x - m) / jnp.sqrt(v + eps)

def _scatter_add(tgt, idx, src, axis=0):
    return tgt.at[idx].add(src)

def _segment_sum(src, seg, n):
    return jax.ops.segment_sum(src, seg, n)
kernel_name = 'mk_adaln_ffn_d2_seqx_r4_a31d63'

def setup_inputs(seed: int=0):
    np.random.seed(seed)
    _w = jnp.asarray

    def _rec_inputs():
        import jax
        import jax.numpy as jnp
        _rk = jax.random.key(seed)
        x = -7.109e-05 + 0.9999 * jax.random.normal(jax.random.fold_in(_rk, 1), (32, 64, 1024), jnp.float32)
        _lenS = 64 - jax.random.randint(jax.random.fold_in(_rk, 7), (32,), 0, max(1, 64 // 4) + 1, jnp.int32)
        _lenS2 = 64 - jax.random.randint(jax.random.fold_in(_rk, 8), (32,), 0, max(1, 64 // 4) + 1, jnp.int32)
        itok_B_0_15 = jax.random.randint(jax.random.fold_in(_rk, 11), (32,), 0, 16, jnp.int32)
        return (x, itok_B_0_15)
    x, itok_B_0_15 = _rec_inputs()

    def _L0_cond_setup():
        import jax, jax.numpy as jnp
        import numpy as np
        NUM_CONDITIONS = 16
        IN_CH = 64
        OUT_CH = 64
        B = 64
        T = 1024
        key = jax.random.key(seed)
        k_x, k_w, k_c = jax.random.split(key, 3)
        x = jax.random.normal(k_x, (B, IN_CH, T), dtype=jnp.float32)
        bound = float(np.sqrt(6.0 / IN_CH))
        weights = jax.random.uniform(k_w, (NUM_CONDITIONS, IN_CH, OUT_CH), dtype=jnp.float32, minval=-bound, maxval=bound)
        condition = jax.random.randint(k_c, (B,), 0, NUM_CONDITIONS, dtype=jnp.int64)
        return {'x': x, 'weights': weights, 'condition': condition}
    _L0_cond_all = _L0_cond_setup()
    _L0_cond_in = {k: v for k, v in _L0_cond_all.items() if k in ('weights',)}
    del _L0_cond_all

    def _L0_ffn_setup():
        import jax, jax.numpy as jnp
        import numpy as np
        M = 1024
        K = 1024

        def _make_2to4_mask(key, shape):
            scores = jax.random.normal(key, shape)
            g = scores.reshape(shape[0], shape[1] // 4, 4)
            rank = jnp.argsort(jnp.argsort(-jnp.abs(g), axis=-1), axis=-1)
            return (rank < 2).reshape(shape).astype(jnp.float32)
        key = jax.random.key(seed)
        k_x, k_w12, k_b12, k_w3, k_b3, k_m = jax.random.split(key, 6)
        x = jax.random.normal(k_x, (4, 512, K), dtype=jnp.float32)
        w12_dense = jax.random.normal(k_w12, (2 * M, K), dtype=jnp.float32) * (1.0 / np.sqrt(K))
        mask12 = _make_2to4_mask(k_m, (2 * M, K))
        w12 = w12_dense * mask12
        b12 = jax.random.normal(k_b12, (2 * M,), dtype=jnp.float32) * 0.01
        w3 = jax.random.normal(k_w3, (M, M), dtype=jnp.float32) * (1.0 / np.sqrt(M))
        b3 = jax.random.normal(k_b3, (M,), dtype=jnp.float32) * 0.01
        return {'x': x, 'w12': w12, 'b12': b12, 'w3': w3, 'b3': b3}
    _L0_ffn_all = _L0_ffn_setup()
    _L0_ffn_in = {k: v for k, v in _L0_ffn_all.items() if k in ('w12', 'b12', 'w3', 'b3')}
    del _L0_ffn_all

    def _L1_cond_setup():
        import jax, jax.numpy as jnp
        import numpy as np
        SCALING = 16.0 / 16
        key = jax.random.key(seed)
        k1, k2, k3, k4, k5 = jax.random.split(key, 5)
        B, S, D_IN, D_OUT, R, N_ADPT = (8, 512, 1024, 1024, 16, 16)
        x = jax.random.normal(k1, (B, S, D_IN), dtype=jnp.float32)
        adapter_indices = jax.random.randint(k2, (B,), 0, N_ADPT, dtype=jnp.int32)
        W = jax.random.normal(k3, (D_IN, D_OUT), dtype=jnp.float32) * 0.02
        lora_A = jax.random.normal(k4, (N_ADPT, D_IN, R), dtype=jnp.float32) * 0.02
        lora_B = jax.random.normal(k5, (N_ADPT, R, D_OUT), dtype=jnp.float32) * 0.02
        return {'x': x, 'adapter_indices': adapter_indices, 'W': W, 'lora_A': lora_A, 'lora_B': lora_B}
    _L1_cond_all = _L1_cond_setup()
    _L1_cond_in = {k: v for k, v in _L1_cond_all.items() if k in ('W', 'lora_A', 'lora_B')}
    del _L1_cond_all

    def _L1_ffn_setup():
        import jax, jax.numpy as jnp
        import numpy as np
        import math
        B, S, IN, OUT = (4, 512, 1024, 1024)
        E, R, K = (8, 64, 128)
        SCALE = 64.0 / 64.0
        MULTIPLIER = 1.0
        key = jax.random.key(seed)
        ks = jax.random.split(key, 6)
        return {'x': jax.random.normal(ks[0], (B, S, IN), jnp.float32), 'W_org': jax.random.normal(ks[1], (OUT, IN), jnp.float32) * 0.02, 'lora_down': jax.random.normal(ks[2], (E, IN, R), jnp.float32) * 0.02, 'lora_up': jax.random.normal(ks[3], (E, R, OUT), jnp.float32) * 0.02, 'lora_keys': jax.random.normal(ks[4], (E, K), jnp.float32), 'Wq': jax.random.normal(ks[5], (K, IN), jnp.float32) * 0.02}
    _L1_ffn_all = _L1_ffn_setup()
    _L1_ffn_in = {k: v for k, v in _L1_ffn_all.items() if k in ('W_org', 'lora_down', 'lora_up', 'lora_keys', 'Wq')}
    del _L1_ffn_all
    return {'x': x, 'itok_B_0_15': itok_B_0_15, 'L0_cond_weights': _L0_cond_in['weights'], 'L0_ffn_w12': _L0_ffn_in['w12'], 'L0_ffn_b12': _L0_ffn_in['b12'], 'L0_ffn_w3': _L0_ffn_in['w3'], 'L0_ffn_b3': _L0_ffn_in['b3'], 'L1_cond_W': _L1_cond_in['W'], 'L1_cond_lora_A': _L1_cond_in['lora_A'], 'L1_cond_lora_B': _L1_cond_in['lora_B'], 'L1_ffn_W_org': _L1_ffn_in['W_org'], 'L1_ffn_lora_down': _L1_ffn_in['lora_down'], 'L1_ffn_lora_up': _L1_ffn_in['lora_up'], 'L1_ffn_lora_keys': _L1_ffn_in['lora_keys'], 'L1_ffn_Wq': _L1_ffn_in['Wq']}

def reference(x, itok_B_0_15, L0_cond_weights, L0_ffn_w12, L0_ffn_b12, L0_ffn_w3, L0_ffn_b3, L1_cond_W, L1_cond_lora_A, L1_cond_lora_B, L1_ffn_W_org, L1_ffn_lora_down, L1_ffn_lora_up, L1_ffn_lora_keys, L1_ffn_Wq):
    import jax
    import jax.numpy as jnp

    def _L0_cond_ref(x, weights, condition):
        import jax, jax.numpy as jnp
        import numpy as np
        NUM_CONDITIONS = 16
        IN_CH = 64
        OUT_CH = 64
        B = 64
        T = 1024
        W = weights[condition]
        return jnp.einsum('bct,bcd->bdt', x, W)

    def _L0_ffn_ref(x, w12, b12, w3, b3):
        import jax, jax.numpy as jnp
        import numpy as np
        M = 1024
        K = 1024

        def _make_2to4_mask(key, shape):
            scores = jax.random.normal(key, shape)
            g = scores.reshape(shape[0], shape[1] // 4, 4)
            rank = jnp.argsort(jnp.argsort(-jnp.abs(g), axis=-1), axis=-1)
            return (rank < 2).reshape(shape).astype(jnp.float32)
        x12 = jnp.einsum('bsk,mk->bsm', x, w12) + b12
        x1, x2 = jnp.split(x12, 2, axis=-1)
        x4 = jax.nn.silu(x1) * x2
        return jnp.einsum('bsm,nm->bsn', x4, w3) + b3

    def _L1_cond_ref(x, adapter_indices, W, lora_A, lora_B):
        import jax, jax.numpy as jnp
        import numpy as np
        SCALING = 16.0 / 16
        base_out = jnp.einsum('bsi,io->bso', x, W)
        A = lora_A[adapter_indices]
        Bm = lora_B[adapter_indices]
        xr = jnp.einsum('bsi,bir->bsr', x, A)
        lora_out = jnp.einsum('bsr,bro->bso', xr, Bm)
        return base_out + lora_out * SCALING

    def _L1_ffn_ref(x, W_org, lora_down, lora_up, lora_keys, Wq):
        import jax, jax.numpy as jnp
        import numpy as np
        import math
        B, S, IN, OUT = (4, 512, 1024, 1024)
        E, R, K = (8, 64, 128)
        SCALE = 64.0 / 64.0
        MULTIPLIER = 1.0
        base = jnp.einsum('bsi,oi->bso', x, W_org)
        q = jnp.einsum('bi,ki->bk', x.mean(axis=1), Wq)
        scores = jnp.einsum('bk,ek->be', q, lora_keys) / math.sqrt(K)
        coeffs = jax.nn.softmax(scores, axis=-1)
        h = jnp.einsum('bsi,eir->bser', x, lora_down)
        delta = jnp.einsum('be,bser,ero->bso', coeffs, h, lora_up)
        return base + delta * (SCALE * MULTIPLIER)
    x = x + _L0_ffn_ref(_L0_cond_ref(x, L0_cond_weights, itok_B_0_15), L0_ffn_w12, L0_ffn_b12, L0_ffn_w3, L0_ffn_b3)
    x = x + _L1_ffn_ref(_L1_cond_ref(x, itok_B_0_15, L1_cond_W, L1_cond_lora_A, L1_cond_lora_B), L1_ffn_W_org, L1_ffn_lora_down, L1_ffn_lora_up, L1_ffn_lora_keys, L1_ffn_Wq)
    return x

_drawn_inputs = setup_inputs


def setup_inputs(seed=0):
    import zlib

    import numpy as np

    out = dict(_drawn_inputs(seed))
    spreads = {}
    factors = {'L0_ffn_b12': 7.104, 'L0_ffn_b3': 7.284, 'L1_ffn_lora_keys': 8.0, 'L1_ffn_Wq': 8.0}
    for name, (base, spread) in spreads.items():
        noise = np.random.default_rng([zlib.crc32(name.encode()), seed]).standard_normal(out[name].shape)
        drawn = base * np.exp(spread * noise) if base else spread * noise
        out[name] = jnp.asarray(drawn.astype(out[name].dtype))
    for name, factor in factors.items():
        out[name] = (out[name] * factor).astype(out[name].dtype)
    return out
```

```python
from contextlib import ExitStack

import concourse.bass as bass
from concourse import mybir
from concourse.alu_op_type import AluOpType as ALU

F32 = mybir.dt.float32
F32R = mybir.dt.float32r
I32 = mybir.dt.int32
ACT = mybir.ActivationFunctionType
AX_X = mybir.AxisListType.X

P = 128
B, S, D = 32, 64, 1024
K = D // P
HALVES = 2
TOK = B * S // HALVES
TN = 512
TILES = TOK // TN
BT = TN // S
BH = TOK // S
PAIRS = BH // 2
RANK = 16
E, ER = 8, 64
KE = E * ER // P
NCOND = 16
SHARE = 6

UPGATE = 0
DOWN = UPGATE + 2 * K
LORA_A = DOWN + K
LINEAR = LORA_A + TILES
EXPERT_IN = LINEAR + K
FINAL = EXPERT_IN + KE
UNITS = FINAL + K + K // 2
USES = UNITS // 2
LOADS = USES - 1

BANK_USES = [22, 22, 21, 21, 2, 2]
FULLS = [22, 4, 21, 0, 1]
USE_UPGATE, USE_DOWN, USE_LINEAR, USE_EXPERT = 0, 8, 12, 16
USE_FINAL = [18, 18, 17, 17]
EXPERT_BANK = [0, 2, 4, 0]
EXPERT_USE = [16, 16, 1, 17]
EXPERT_FILL = [17, 17, 1, 18]
FINAL_FILL = [19, 1, 18]
KEY = 128
SCORE_SCALE = 1.0 / (S * KEY ** 0.5)
USE_XR = 0


def build(nc, x_pairs, x_t, idx, cond_w, w_upgate, b_upgate, w_down, b_down,
          w_linear, lora_a, lora_b, w_org, exp_in, exp_out, keys_t, wq_t, out_t):
    with ExitStack() as ctx:
        def sb(name, shape, dt=F32):
            return ctx.enter_context(nc.sbuf_tensor(name, shape, dt))

        def sem(name):
            return ctx.enter_context(nc.semaphore(name))

        even_hi, even_lo = sb("even_hi", [P, K, TOK], F32R), sb("even_lo", [P, K, TOK], F32R)
        odd_hi, odd_lo = sb("odd_hi", [P, K, TOK], F32R), sb("odd_lo", [P, K, TOK], F32R)
        inner = sb("inner", [P, 2, KE, TOK], F32R)
        g_hi, g_lo = inner[:, 0], inner[:, 1]
        xr = inner[:, :, 0]
        bs = inner[:, :, 1, 0:2 * TILES * P].rearrange("p h (s t m) -> p h s t m", s=2, t=TILES)
        w_hi, w_lo = sb("w_hi", [P, 2, K, P], F32R), sb("w_lo", [P, 2, K, P], F32R)
        w_raw = sb("w_raw", [P, 2, K * P])
        x_raw = sb("x_raw", [P, 2, K * P])
        gathered = sb("gathered", [P, TILES, D])
        x_slots = [x_raw[:, 0, :], x_raw[:, 1, :], gathered[:, 0, :], gathered[:, 1, :]]
        mix = sb("mix", [P, PAIRS, P])
        work = sb("work", [P, 4, TN])
        idx_sb = sb("idx_sb", [1, B + BH], I32)
        b_up_sb = sb("b_up_sb", [P, 2 * K])
        b_dn_sb = sb("b_dn_sb", [P, K])
        keys_sb = sb("keys_sb", [P, E])
        mask = sb("mask", [P, BT])
        ident = sb("ident", [BH, BH])
        y_sum = sb("y_sum", [P, K, BH])
        q_sb = sb("q_sb", [P, BH])
        smax, sbias = sb("smax", [BH, 1]), sb("sbias", [BH, 1])
        ssum, sinv = sb("ssum", [BH, 1]), sb("sinv", [BH, 1])
        sexp = sb("sexp", [BH, E])
        coef_rows = sb("coef_rows", [BH, E, ER])
        coef = sb("coef", [P, KE, BH])

        banks = ctx.enter_context(nc.psum_tensor("banks", [P, 8, TN], F32))
        mixed = [banks[:, 4 + 2 * j:6 + 2 * j, :].rearrange("p a (c m) -> p (a c) m", m=P) for j in range(2)]
        router = banks[:, 7, :]

        small_loaded = sem("small_loaded")
        idx_loaded = sem("idx_loaded")
        mix_zeroed = sem("mix_zeroed")
        consts_made = sem("consts_made")
        raw_loaded = [sem(f"raw_loaded{s}") for s in range(2)]
        x_loaded = [sem(f"x_loaded{c}") for c in range(4)]
        a_gathered = [sem(f"a_gathered{s}") for s in range(2)]
        w_hi_done = [sem(f"w_hi_done{s}") for s in range(2)]
        w_ready = [sem(f"w_ready{s}") for s in range(2)]
        unit_done = [sem(f"unit_done{s}") for s in range(2)]
        cond_gathered = sem("cond_gathered")
        cond_begun = sem("cond_begun")
        b_gathered = sem("b_gathered")
        b_hi_done = sem("b_hi_done")
        b_split = sem("b_split")
        wq_loaded = sem("wq_loaded")
        mixed_full = [sem(f"mixed_full{j}") for j in range(2)]
        h_hi_done = sem("h_hi_done")
        h_ready = [sem(f"h_ready{j}") for j in range(2)]
        bank_full = [sem(f"bank_full{b}") for b in range(5)]
        bank_free = [sem(f"bank_free{b}") for b in range(6)]
        gated_hi_done = [sem(f"gated_hi_done{t}") for t in range(TILES)]
        gated_ready = [sem(f"gated_ready{t}") for t in range(TILES)]
        xres_loaded = [sem(f"xres_loaded{t}") for t in range(TILES)]
        x1_hi_done = [sem(f"x1_hi_done{t}") for t in range(TILES)]
        x1_ready = [sem(f"x1_ready{t}") for t in range(TILES)]
        xr_hi_done = [sem(f"xr_hi_done{t}") for t in range(TILES)]
        xr_ready = [sem(f"xr_ready{t}") for t in range(TILES)]
        y_hi_done = [sem(f"y_hi_done{t}") for t in range(TILES)]
        g_hi_done = [sem(f"g_hi_done{t}") for t in range(TILES)]
        g_ready = [sem(f"g_ready{t}") for t in range(TILES)]
        q_full = sem("q_full")
        q_copied = sem("q_copied")
        scores_full = sem("scores_full")
        max_done = sem("max_done")
        bias_done = sem("bias_done")
        exp_done = sem("exp_done")
        inv_done = sem("inv_done")
        rows_done = sem("rows_done")
        coef_full = sem("coef_full")
        coef_ready = sem("coef_ready")
        out_ready = [sem(f"out_ready{b}") for b in range(4)]
        out_stored = [sem(f"out_stored{b}") for b in range(4)]
        stored = [sem(f"stored{b}") for b in range(4)]

        passed = sem("passed")

        FIRST = 1

        def start_from_one(eng, semaphores):
            for semaphore in semaphores:
                eng.sem_inc(semaphore, FIRST)

        def wait_alone(eng, semaphore, count):
            eng.wait_ge(semaphore, count)
            eng.sem_inc(passed, 1)

        def use(h, u):
            return h * USES + u

        def load_count(h, pair, gather_seen):
            return h * LOADS + pair + 1 - gather_seen

        def tok(t):
            return slice(t * TN, (t + 1) * TN)

        def wait_group(eng, h, b, s, fills, pair):
            if b % 2 == 0:
                eng.wait_ge(bank_full[b], h * FULLS[b] + fills)
            else:
                eng.wait_ge(unit_done[s], FIRST + use(h, pair) + 1)

        def in_order(unit):
            return unit.rearrange("p k m -> p (k m)")

        def as_gathered(raw):
            return raw.rearrange("p (b k r) -> p b k r", k=K, r=RANK)

        def of_gather(unit):
            return unit.rearrange("p k (b r) -> p b k r", r=RANK)

        def chunk(buf, k, t):
            return buf[:, bass.ds(k, 1), tok(t)].rearrange("p a n -> p (a n)")

        def gather_mixing(eng, half, js, semaphore, pairs=(0, PAIRS)):
            with eng.Fori(*pairs) as pair:
                for j in js:
                    v = eng.value_load(idx_sb[0:1, bass.ds(half * BH + pair * 2 + j, 1)],
                                       min_val=0, max_val=NCOND - 1)
                    r = slice(j * S, (j + 1) * S)
                    eng.dma_start(mix[r, bass.ds(pair, 1), r].rearrange("p a m -> p (a m)"),
                                  cond_w[v]).then_inc(semaphore, 16)

        def sync_engine(sp):
            sp.dma_start(idx_sb[:, 0:B], idx).then_inc(idx_loaded, 16)
            sp.dma_start(idx_sb[:, B:B + BH], idx[:, 0:BH]).then_inc(idx_loaded, 16)
            sp.wait_ge(idx_loaded, 32)
            sp.wait_ge(mix_zeroed, 1)
            gather_mixing(sp, 0, (0, 1), cond_begun, (SHARE, PAIRS))

            def load(h, pair, s, src, seen):
                sp.wait_ge(w_ready[s], FIRST + use(h, pair))
                sp.dma_start(w_raw[:, s, :], src).then_inc(raw_loaded[s], 16)

            def half(h):
                for s in range(2):
                    load(h, UPGATE // 2, s, w_upgate[s], 0)
                wait_alone(sp, q_full, FIRST + h)
                wait_alone(sp, b_split, FIRST + h * K)
                with sp.Fori(0, PAIRS // 4) as q:
                    for c in range(4):
                        sp.wait_ge(mixed_full[c % 2], FIRST + h * (PAIRS // 2) + q * (1 + c // 2))
                        sp.dma_start(x_slots[c], x_pairs[h * PAIRS + q * 4 + c]).then_inc(x_loaded[c], 16)
                with sp.Fori(1, K) as m:
                    for s in range(2):
                        load(h, UPGATE // 2 + m, s, w_upgate[m * 2 + s], 0)
                with sp.Fori(0, K // 2) as i:
                    for s in range(2):
                        load(h, DOWN // 2 + i, s, w_down[i * 2 + s], 0)
                sp.wait_ge(idx_loaded, 32)
                for t in range(TILES):
                    wait_alone(sp, w_ready[t], FIRST + use(h, LORA_A // 2))
                    with sp.Fori(0, BT) as b:
                        v = sp.value_load(idx_sb[0:1, bass.ds(h * BH + t * BT + b, 1)],
                                          min_val=0, max_val=NCOND - 1)
                        sp.dma_start(w_raw[:, t, bass.ds(b * P, P)], lora_a[v]).then_inc(a_gathered[t], 16)
                with sp.Fori(0, K // 2) as i:
                    for s in range(2):
                        load(h, LINEAR // 2 + i, s, w_linear[i * 2 + s], 1)
                for s in range(2):
                    load(h, EXPERT_IN // 2, s, exp_in[s], 1)
                sp.wait_ge(b_split, FIRST + (h + 1) * K)
                sp.dma_start(gathered[:, 0, :], wq_t).then_inc(wq_loaded, 16)
                for s in range(2):
                    load(h, EXPERT_IN // 2 + 1, s, exp_in[2 + s], 1)
                with sp.Fori(0, 2) as q:
                    srcs = [w_org[q * 4], w_org[q * 4 + 1], exp_out[q * 2],
                            w_org[q * 4 + 2], w_org[q * 4 + 3], exp_out[q * 2 + 1]]
                    for j, src in enumerate(srcs):
                        load(h, FINAL // 2 + q * 3 + j // 2, j % 2, src, 1)

            with sp.Fori(0, HALVES) as h:
                half(h)
            load(HALVES, 0, 0, w_upgate[0], 0)

        def pool_engine(pool):
            start_from_one(pool, stored)
            pool.wait_ge(idx_loaded, 32)
            pool.wait_ge(mix_zeroed, 1)
            gather_mixing(pool, 0, (1,), cond_gathered, (0, SHARE))
            for dst, src in ((b_up_sb, b_upgate), (b_dn_sb, b_down), (keys_sb, keys_t)):
                pool.dma_start(dst[:, :], src).then_inc(small_loaded, 16)
            pool.memset(mask[:, :], 1.0).then_inc(consts_made, 1)
            pool.memset(ident[:, :], 0.0).then_inc(consts_made, 1)
            pool.wait_ge(consts_made, 2)
            pool.affine_select(out=mask[:, :], in_=mask[:, :], compare_op=ALU.is_ge, fill=0.0, base=0,
                               pattern=[[-RANK, BT]], channel_multiplier=1).then_inc(consts_made, 1)
            pool.wait_ge(consts_made, 3)
            pool.affine_select(out=mask[:, :], in_=mask[:, :], compare_op=ALU.is_ge, fill=0.0, base=RANK - 1,
                               pattern=[[RANK, BT]], channel_multiplier=-1).then_inc(consts_made, 1)
            pool.affine_select(out=ident[:, :], in_=ident[:, :], compare_op=ALU.not_equal, fill=1.0, base=0,
                               pattern=[[-1, BH]], channel_multiplier=1).then_inc(consts_made, 1)

            def load_xres(h, n, t):
                pool.dma_start(work[:, t, :], x_t[n, :, bass.ds(h * TOK + t * TN, TN)]).then_inc(
                    xres_loaded[t], 16)

            def half(h):
                for j in range(2):
                    wait_alone(pool, mixed_full[j], FIRST + (h + 1) * (PAIRS // 2))
                for b in range(BH):
                    v = pool.value_load(idx_sb[0:1, bass.ds(h * BH + b, 1)], min_val=0, max_val=NCOND - 1)
                    r = (b % BT) * RANK
                    pool.dma_start(gathered[r:r + RANK, b // BT, :], lora_b[v]).then_inc(b_gathered, 16)
                gather_mixing(pool, h + 1, (0, 1), cond_gathered)
                for t in range(TILES):
                    pool.wait_ge(bank_free[2 + t], FIRST + h * BANK_USES[2] + USE_DOWN)
                    load_xres(h, 0, t)
                with pool.Fori(0, K // 2 - 1) as i:
                    for j in range(2):
                        for t in range(TILES):
                            b = 2 * j + t
                            pool.wait_ge(bank_free[b], FIRST + h * BANK_USES[b] + USE_DOWN + i + 1)
                            load_xres(h, i * 2 + j + 1, t)
                for t in range(TILES):
                    pool.wait_ge(bank_free[t], FIRST + h * BANK_USES[t] + USE_DOWN + K // 2)
                    load_xres(h, K - 1, t)
                with pool.Fori(0, K // 2) as i:
                    for b in range(4):
                        pool.wait_ge(out_ready[b], h * (K // 2) + i + 1)
                        pool.dma_start(out_t[i * 2 + b // 2, :, bass.ds(h * TOK + (b % 2) * TN, TN)],
                                       work[:, b, :]).then_inc(out_stored[b], 16)
                    for b in range(4):
                        pool.wait_ge(out_stored[b], (h * (K // 2) + i + 1) * 16)
                        pool.sem_inc(stored[b], 1)

            with pool.Fori(0, HALVES) as h:
                half(h)

        def tensor_engine(pe):
            start_from_one(pe, unit_done + mixed_full + [q_full])

            def product(out, stat_hi, stat_lo, mov_hi, mov_lo, start, stop):
                pe.matmul(out, stat_hi, mov_hi, start=start, stop=False)
                pe.matmul(out, stat_hi, mov_lo, start=False, stop=False)
                return pe.matmul(out, stat_lo, mov_hi, start=False, stop=stop)

            def chunks(b, s, hi, lo, t, count=K, tile0=0, start=True, stop=True, last_wait=None):
                for k in range(count):
                    if k == count - 1 and last_wait is not None:
                        last_wait()
                    last = product(banks[:, b, :], w_hi[:, s, tile0 + k, :], w_lo[:, s, tile0 + k, :],
                                   hi[:, k, tok(t)], lo[:, k, tok(t)],
                                   start and k == 0, stop and k == count - 1)
                return last

            def half(h):
                wait_alone(pe, cond_gathered, (h * BH + SHARE) * 16)
                with pe.Fori(0, PAIRS // 4) as q:
                    for c in range(4):
                        j, i = c % 2, q * 2 + c // 2
                        pe.wait_ge(x_loaded[c], (h * (PAIRS // 4) + q + 1) * 16)
                        pe.wait_ge(h_ready[j], FIRST + h * (PAIRS // 2) + i)
                        matrix = mix[:, bass.ds(q * 4 + c, 1), :].rearrange("p a m -> p (a m)")
                        for k in range(K):
                            last = pe.matmul(mixed[j][:, k, :], x_slots[c][:, k * P:(k + 1) * P], matrix,
                                             start=True, stop=True)
                        last.then_inc(mixed_full[j], 1)
                with pe.Fori(0, K) as m:
                    for s in range(2):
                        pe.wait_ge(w_ready[s], FIRST + use(h, UPGATE // 2 + m) + 1)
                        for t in range(TILES):
                            b = 2 * s + t
                            for j in range(2):
                                pe.wait_ge(h_ready[j], FIRST + h * (PAIRS // 2) + (t + 1) * (PAIRS // 4))
                            pe.wait_ge(bank_free[b], FIRST + h * BANK_USES[b] + USE_UPGATE + m)
                            chunks(b, s, even_hi, even_lo, t).then_inc(unit_done[s] if t else bank_full[b], 1)
                with pe.Fori(0, K // 2) as i:
                    for s in range(2):
                        pe.wait_ge(w_ready[s], FIRST + use(h, DOWN // 2 + i) + 1)
                        for t in range(TILES):
                            b = 2 * s + t
                            pe.wait_ge(bank_free[b], FIRST + h * BANK_USES[b] + USE_DOWN + i)
                            pe.wait_ge(gated_ready[t], h * K + K - 1)
                            chunks(b, s, odd_hi, odd_lo, t,
                                   last_wait=lambda: pe.wait_ge(gated_ready[t], h * K + K),
                                   ).then_inc(unit_done[s] if t else bank_full[b], 1)
                for t in range(TILES):
                    pe.wait_ge(w_ready[t], FIRST + use(h, LORA_A // 2) + 1)
                    pe.wait_ge(x1_ready[t], h * K + K - 1)
                    chunks(4 + t, t, even_hi, even_lo, t,
                           last_wait=lambda: pe.wait_ge(x1_ready[t], h * K + K),
                           ).then_inc(unit_done[t], 1)
                with pe.Fori(0, K // 2) as i:
                    for s in range(2):
                        pe.wait_ge(w_ready[s], FIRST + use(h, LINEAR // 2 + i) + 1)
                        for t in range(TILES):
                            b = 2 * s + t
                            pe.wait_ge(bank_free[b], FIRST + h * BANK_USES[b] + USE_LINEAR + i)
                            chunks(b, s, even_hi, even_lo, t, stop=False)
                            pe.wait_ge(xr_ready[t], h + 1)
                            product(banks[:, b, :], bs[:, 0, s, t], bs[:, 1, s, t], xr[:, 0, tok(t)],
                                    xr[:, 1, tok(t)], False, True).then_inc(unit_done[s] if t else bank_full[b], 1)
                for e in range(KE):
                    s = e % 2
                    pe.wait_ge(w_ready[s], FIRST + use(h, EXPERT_IN // 2 + e // 2) + 1)
                    for t in range(TILES):
                        b = EXPERT_BANK[e] + t
                        if e in (0, 1, 3):
                            pe.wait_ge(bank_free[b], FIRST + h * BANK_USES[b] + EXPERT_USE[e])
                        pe.wait_ge(bank_free[t], FIRST + h * BANK_USES[t] + USE_EXPERT)
                        chunks(b, s, odd_hi, odd_lo, t,
                               last_wait=lambda: pe.wait_ge(bank_free[2 + t], FIRST + h * BANK_USES[2] + USE_EXPERT),
                               ).then_inc(unit_done[s] if t else bank_full[b], 1)
                        if e == 1 and t == 0:
                            pe.wait_ge(q_copied, h + 1)
                            pe.wait_ge(small_loaded, 48)
                            pe.matmul(router[0:BH, 32:32 + E], q_sb[:, :], keys_sb[:, :],
                                      start=True, stop=True).then_inc(scores_full, 1)
                    if e == 0:
                        pe.wait_ge(wq_loaded, (h + 1) * 16)
                        for k in range(K):
                            last = pe.matmul(router[:, 0:BH], gathered[:, 0, k * P:(k + 1) * P],
                                             y_sum[:, k, :], start=(k == 0), stop=(k == K - 1))
                        last.then_inc(q_full, 1)
                    if e == 1:
                        pe.wait_ge(rows_done, h + 1)
                        pe.wait_ge(consts_made, 5)
                        for k in range(KE):
                            rows = coef_rows[:, 2 * k:2 * k + 2, :].rearrange("b e r -> b (e r)")
                            last = pe.matmul(router[:, 64 + k * BH:64 + (k + 1) * BH], rows, ident[:, :],
                                             start=True, stop=True)
                        last.then_inc(coef_full, 1)
                with pe.Fori(0, 2) as q:
                    for j in range(6):
                        s = j % 2
                        pe.wait_ge(w_ready[s], FIRST + use(h, FINAL // 2 + q * 3 + j // 2) + 1)
                        if j % 3 < 2:
                            for t in range(TILES):
                                b = 2 * (j % 3) + t
                                pe.wait_ge(bank_free[b], FIRST + h * BANK_USES[b] + USE_FINAL[b] + q * 2 + j // 3)
                                last = chunks(b, s, odd_hi, odd_lo, t, stop=False)
                            if t == TILES - 1:
                                last.then_inc(unit_done[s], 1)
                        else:
                            for b in range(4):
                                pe.wait_ge(g_ready[b % 2], (h + 1) * KE)
                                last = chunks(b, s, g_hi, g_lo, b % 2, count=KE, tile0=KE * (b // 2),
                                              start=False)
                                last.then_inc(unit_done[s] if b == 3 else bank_full[b], 1)

            pe.wait_ge(cond_begun, (2 * PAIRS - SHARE) * 16)
            with pe.Fori(0, HALVES) as h:
                half(h)

        def scalar_engine(act):
            def split(h, pair, s, seen=0, gather=False):
                raw = w_raw[:, s, :]
                if gather:
                    act.wait_ge(a_gathered[s], (h + 1) * BT * 16)
                else:
                    act.wait_ge(raw_loaded[s], load_count(h, pair, seen) * 16)
                act.wait_ge(unit_done[s], FIRST + use(h, pair))
                hi = w_hi[:, s, :, :]
                act.copy(of_gather(hi) if gather else in_order(hi), as_gathered(raw) if gather else raw
                         ).then_inc(w_hi_done[s], 1)

            def half(h):
                act.wait_ge(bank_free[3], FIRST + h * BANK_USES[3])
                with act.Fori(0, PAIRS // 2) as i:
                    for j in range(2):
                        act.wait_ge(mixed_full[j], FIRST + h * (PAIRS // 2) + i + 1)
                        act.copy(even_hi[:, :, bass.ds((i * 2 + j) * P, P)], mixed[j]).then_inc(h_hi_done, 1)
                for t in range(TILES):
                    act.wait_ge(stored[t], FIRST + h * (K // 2))
                act.wait_ge(small_loaded, 48)
                with act.Fori(0, K) as m:
                    split(h, UPGATE // 2 + m, 1)
                    for t in range(TILES):
                        wait_group(act, h, t, 0, USE_UPGATE + m + 1, UPGATE // 2 + m)
                        act.sem_inc(passed, 1)
                        act.activation(work[:, t, :], banks[:, t, :], ACT.Silu,
                                       bias=b_up_sb[:, bass.ds(m, 1)]).then_inc(bank_free[t], 1)
                    split(h, UPGATE // 2 + m + 1, 0)
                    for t in range(TILES):
                        act.wait_ge(bank_free[2 + t], FIRST + h * BANK_USES[2] + USE_UPGATE + m + 1)
                        act.copy(chunk(odd_hi, m, t),
                                 work[:, 2 + t, :]).then_inc(gated_hi_done[t], 1)

                def down(i, last):
                    for s in range(2):
                        if s == 0:
                            split(h, DOWN // 2 + i, 1)
                        else:
                            split(h, DOWN // 2 + i + 1, 0, gather=last)
                        for t in range(TILES):
                            b = 2 * s + t
                            act.wait_ge(bank_free[b], FIRST + h * BANK_USES[b] + USE_DOWN + i + 1)
                            act.copy(chunk(even_hi, i * 2 + s, t),
                                     work[:, 2 + t, :]).then_inc(x1_hi_done[t], 1)

                with act.Fori(0, K // 2 - 1) as i:
                    down(i, False)
                down(K // 2 - 1, True)

                def split_linear(pair, s, n):
                    act.wait_ge(unit_done[s], FIRST + use(h, pair))
                    act.copy(bs[:, 0, s], gathered[:, :, bass.ds(n * P, P)]).then_inc(b_hi_done, 1)
                    split(h, pair, s, seen=1)

                act.wait_ge(b_gathered, (h + 1) * BH * 16)
                split(h, LORA_A // 2, 1, gather=True)
                for t in range(TILES):
                    if t == 1:
                        split_linear(LINEAR // 2, 0, 0)
                    act.wait_ge(bank_free[4 + t], FIRST + h * BANK_USES[4] + USE_XR + 1)
                    act.copy(xr[:, 0, tok(t)], work[:, 2 + t, :]).then_inc(xr_hi_done[t], 1)

                def linear(i, last):
                    for s in range(2):
                        if s == 0:
                            split_linear(LINEAR // 2 + i, 1, i * 2 + 1)
                        elif not last:
                            split_linear(LINEAR // 2 + i + 1, 0, i * 2 + 2)
                        else:
                            split(h, EXPERT_IN // 2, 0, seen=1)
                        for t in range(TILES):
                            b = 2 * s + t
                            wait_group(act, h, b, s, USE_LINEAR + i + 1, LINEAR // 2 + i)
                            act.copy(chunk(odd_hi, i * 2 + s, t),
                                     banks[:, b, :]).then_inc(y_hi_done[t], 1)

                with act.Fori(0, K // 2 - 1) as i:
                    linear(i, False)
                linear(K // 2 - 1, True)

                split(h, EXPERT_IN // 2, 1, seen=1)
                split(h, EXPERT_IN // 2 + 1, 0, seen=1)
                act.wait_ge(bias_done, h + 1)
                act.activation(sexp[:, :], router[0:BH, 32:32 + E], ACT.Exp, bias=sbias[:, :],
                               scale=SCORE_SCALE, accum_out=ssum[:, :]).then_inc(exp_done, 1)

                def expert_hi(e):
                    for t in range(TILES):
                        b = EXPERT_BANK[e] + t
                        act.wait_ge(bank_free[b], FIRST + h * BANK_USES[b] + EXPERT_USE[e] + 1)
                        act.copy(g_hi[:, e, tok(t)], work[:, 2 + t, :]).then_inc(g_hi_done[t], 1)

                expert_hi(0)
                split(h, EXPERT_IN // 2 + 1, 1, seen=1)
                expert_hi(1)
                split(h, FINAL // 2, 0, seen=1)
                expert_hi(2)
                expert_hi(3)
                with act.Fori(0, 2) as q:
                    for j in range(1, 7):
                        split(h, FINAL // 2 + q * 3 + j // 2, j % 2, seen=1)

            act.wait_ge(idx_loaded, 32)
            act.wait_ge(mix_zeroed, 1)
            gather_mixing(act, 0, (0,), cond_begun, (0, SHARE))
            split(0, 0, 0)
            with act.Fori(0, HALVES) as h:
                half(h)

        def vector_engine(dve):
            start_from_one(dve, w_ready + [b_split] + h_ready + bank_free)

            def lo(out, value, hi):
                return dve.tensor_tensor(out, value, hi.bitcast(F32), ALU.subtract)

            def split(h, pair, s, gather=False):
                dve.wait_ge(w_hi_done[s], use(h, pair) + 1)
                raw = w_raw[:, s, :]
                view, raw = (of_gather, as_gathered(raw)) if gather else (in_order, raw)
                lo(view(w_lo[:, s, :, :]), raw, view(w_hi[:, s, :, :])).then_inc(w_ready[s], 1)

            dve.memset(mix[:, :, :], 0.0).then_inc(mix_zeroed, 1)

            def half(h):
                with dve.Fori(0, PAIRS // 2) as i:
                    for j in range(2):
                        dve.wait_ge(h_hi_done, h * PAIRS + i * 2 + j + 1)
                        cols = bass.ds((i * 2 + j) * P, P)
                        lo(even_lo[:, :, cols], mixed[j], even_hi[:, :, cols]).then_inc(h_ready[j], 1)
                for t in range(TILES):
                    wait_alone(dve, stored[2 + t], FIRST + h * (K // 2))
                dve.wait_ge(small_loaded, 48)
                with dve.Fori(0, K) as m:
                    split(h, UPGATE // 2 + m, 1)
                    split(h, UPGATE // 2 + m + 1, 0)
                    for t in range(TILES):
                        dve.wait_ge(bank_free[t], FIRST + h * BANK_USES[t] + USE_UPGATE + m + 1)
                        wait_group(dve, h, 2 + t, 1, USE_UPGATE + m + 1, UPGATE // 2 + m)
                        dve.scalar_tensor_tensor(out=work[:, 2 + t, :], in0=banks[:, 2 + t, :],
                                                 scalar=b_up_sb[:, bass.ds(m + K, 1)], in1=work[:, t, :],
                                                 op0=ALU.add, op1=ALU.mult).then_inc(bank_free[2 + t], 1)
                        dve.wait_ge(gated_hi_done[t], h * K + m + 1)
                        lo(chunk(odd_lo, m, t), work[:, 2 + t, :], chunk(odd_hi, m, t)).then_inc(
                            gated_ready[t], 1)
                def down(i, last):
                    for s in range(2):
                        split(h, DOWN // 2 + i + s, 1 - s, gather=last and s == 1)
                        for t in range(TILES):
                            b, n = 2 * s + t, i * 2 + s
                            wait_group(dve, h, b, s, USE_DOWN + i + 1, DOWN // 2 + i)
                            dve.wait_ge(xres_loaded[t], (h * K + n + 1) * 16)
                            dve.scalar_tensor_tensor(out=work[:, 2 + t, :], in0=banks[:, b, :],
                                                     scalar=b_dn_sb[:, bass.ds(n, 1)], in1=work[:, t, :],
                                                     op0=ALU.add, op1=ALU.add).then_inc(bank_free[b], 1)
                            dve.wait_ge(x1_hi_done[t], h * K + n + 1)
                            lo(chunk(even_lo, n, t), work[:, 2 + t, :], chunk(even_hi, n, t)).then_inc(
                                x1_ready[t], 1)

                with dve.Fori(0, K // 2 - 1) as i:
                    down(i, False)
                down(K // 2 - 1, True)

                def split_linear(pair, s, n):
                    dve.wait_ge(b_hi_done, h * K + n + 1)
                    lo(bs[:, 1, s], gathered[:, :, bass.ds(n * P, P)], bs[:, 0, s]).then_inc(b_split, 1)
                    split(h, pair, s)

                split(h, LORA_A // 2, 1, gather=True)
                dve.wait_ge(consts_made, 5)
                for t in range(TILES):
                    if t == 1:
                        split_linear(LINEAR // 2, 0, 0)
                    dve.wait_ge(unit_done[t], FIRST + use(h, LORA_A // 2) + 1)
                    dve.tensor_tensor(work[:, 2 + t, :].rearrange("p (b n) -> p b n", n=S),
                                      banks[:, 4 + t, :].rearrange("p (b n) -> p b n", n=S),
                                      mask[:, :].unsqueeze(2).to_broadcast([P, BT, S]),
                                      ALU.mult).then_inc(bank_free[4 + t], 1)
                    dve.wait_ge(xr_hi_done[t], h + 1)
                    lo(xr[:, 1, tok(t)], work[:, 2 + t, :], xr[:, 0, tok(t)]).then_inc(xr_ready[t], 1)

                def linear(i, last):
                    for s in range(2):
                        if s == 0:
                            split_linear(LINEAR // 2 + i, 1, i * 2 + 1)
                        elif not last:
                            split_linear(LINEAR // 2 + i + 1, 0, i * 2 + 2)
                        else:
                            split(h, EXPERT_IN // 2, 0)
                        for t in range(TILES):
                            b, n = 2 * s + t, i * 2 + s
                            dve.wait_ge(y_hi_done[t], h * K + n + 1)
                            dve.tensor_reduce(
                                y_sum[:, bass.ds(n, 1), t * BT:(t + 1) * BT].rearrange("p a b -> p (a b)"),
                                banks[:, b, :].rearrange("p (b n) -> p b n", n=S), AX_X, ALU.add)
                            lo(chunk(odd_lo, n, t), banks[:, b, :], chunk(odd_hi, n, t)).then_inc(
                                bank_free[b], 1)

                with dve.Fori(0, K // 2 - 1) as i:
                    linear(i, False)
                linear(K // 2 - 1, True)

                split(h, EXPERT_IN // 2, 1)
                dve.wait_ge(q_full, FIRST + h + 1)
                dve.tensor_copy(q_sb[:, :], router[:, 0:BH]).then_inc(q_copied, 1)
                split(h, EXPERT_IN // 2 + 1, 0)
                dve.wait_ge(scores_full, h + 1)
                dve.reduce_max(smax[:, :], router[0:BH, 32:32 + E], AX_X).then_inc(max_done, 1)
                dve.wait_ge(max_done, h + 1)
                dve.tensor_scalar(sbias[:, :], smax[:, :], -SCORE_SCALE, None, ALU.mult).then_inc(bias_done, 1)
                dve.wait_ge(exp_done, h + 1)
                dve.reciprocal(sinv[:, :], ssum[:, :]).then_inc(inv_done, 1)
                dve.wait_ge(inv_done, h + 1)
                dve.tensor_scalar(coef_rows[:, :, :], sexp[:, :].unsqueeze(2).to_broadcast([BH, E, ER]),
                                  sinv[:, :], None, ALU.mult).then_inc(rows_done, 1)
                dve.wait_ge(coef_full, h + 1)
                dve.tensor_copy(coef[:, :, :].rearrange("p k b -> p (k b)"),
                                router[:, 64:64 + KE * BH]).then_inc(coef_ready, 1)
                dve.wait_ge(coef_ready, h + 1)

                def expert(e):
                    for t in range(TILES):
                        b = EXPERT_BANK[e] + t
                        wait_group(dve, h, b, e % 2, EXPERT_FILL[e], EXPERT_IN // 2 + e // 2)
                        dve.tensor_tensor(work[:, 2 + t, :].rearrange("p (b n) -> p b n", n=S),
                                          banks[:, b, :].rearrange("p (b n) -> p b n", n=S),
                                          coef[:, e, t * BT:(t + 1) * BT].unsqueeze(2).to_broadcast([P, BT, S]),
                                          ALU.mult).then_inc(bank_free[b], 1)
                        dve.wait_ge(g_hi_done[t], h * KE + e + 1)
                        lo(g_lo[:, e, tok(t)], work[:, 2 + t, :], g_hi[:, e, tok(t)]).then_inc(g_ready[t], 1)

                expert(0)
                split(h, EXPERT_IN // 2 + 1, 1)
                expert(1)
                split(h, FINAL // 2, 0)
                expert(2)
                expert(3)
                with dve.Fori(0, 2) as q:
                    for j in range(6):
                        split(h, FINAL // 2 + q * 3 + (j + 1) // 2, (j + 1) % 2)
                        if j % 3 < 2:
                            continue
                        for b in range(4):
                            i, t = q * 2 + j // 3, b % 2
                            n = i * 2 + b // 2
                            if b < 3:
                                dve.wait_ge(bank_full[b], h * FULLS[b] + FINAL_FILL[b] + i)
                            else:
                                dve.wait_ge(unit_done[j % 2], FIRST + use(h, FINAL // 2 + q * 3 + j // 2) + 1)
                            dve.wait_ge(stored[b], FIRST + h * (K // 2) + i)
                            dve.tensor_tensor(work[:, b, :], banks[:, b, :], chunk(even_hi, n, t).bitcast(F32),
                                              ALU.add).then_inc(bank_free[b], 1)
                            dve.wait_ge(bank_free[b], FIRST + h * BANK_USES[b] + USE_FINAL[b] + i + 1)
                            dve.tensor_tensor(work[:, b, :], work[:, b, :], chunk(even_lo, n, t).bitcast(F32),
                                              ALU.add).then_inc(out_ready[b], 1)

            split(0, 0, 0)
            with dve.Fori(0, HALVES) as h:
                half(h)

        with nc.Block() as block:
            @block.sync
            def _(sp):
                sync_engine(sp)

            @block.gpsimd
            def _(pool):
                pool_engine(pool)

            @block.tensor
            def _(pe):
                tensor_engine(pe)

            @block.scalar
            def _(act):
                scalar_engine(act)

            @block.vector
            def _(dve):
                vector_engine(dve)


def kernel(x, itok_B_0_15, L0_cond_weights, L0_ffn_w12, L0_ffn_b12, L0_ffn_w3, L0_ffn_b3,
           L1_cond_W, L1_cond_lora_A, L1_cond_lora_B, L1_ffn_W_org, L1_ffn_lora_down,
           L1_ffn_lora_up, L1_ffn_lora_keys, L1_ffn_Wq):
    import numpy as np
    import concourse.bacc as bacc
    from concourse.bass_utils import run_bass_kernel_spmd

    def units(w):
        w = np.asarray(w)
        n = w.shape[1] // P
        return w.reshape(-1, P, n, P).transpose(2, 1, 0, 3).reshape(n, P, -1)

    x = np.asarray(x)
    w12 = np.asarray(L0_ffn_w12)
    upgate = units(w12.T)
    upgate = upgate.reshape(2, K, P, D).transpose(1, 0, 2, 3).reshape(2 * K, P, D)
    b12 = np.asarray(L0_ffn_b12)
    up = units(np.asarray(L1_ffn_lora_up).reshape(E * ER, D))
    lora_a = np.asarray(L1_cond_lora_A).reshape(NCOND, K, P, RANK).transpose(0, 2, 1, 3)
    ins = {
        "x_pairs": x.reshape(B // 2, P, D),
        "x_t": x.reshape(B * S, K, P).transpose(1, 2, 0),
        "idx": np.asarray(itok_B_0_15).reshape(1, B),
        "cond_w": np.asarray(L0_cond_weights),
        "w_upgate": upgate,
        "b_upgate": b12.reshape(2 * K, P).T,
        "w_down": units(np.asarray(L0_ffn_w3).T),
        "b_down": np.asarray(L0_ffn_b3).reshape(K, P).T,
        "w_linear": units(L1_cond_W),
        "lora_a": lora_a.reshape(NCOND, P, K * RANK),
        "lora_b": np.asarray(L1_cond_lora_B),
        "w_org": units(np.asarray(L1_ffn_W_org).T),
        "exp_in": units(np.asarray(L1_ffn_lora_down).transpose(1, 0, 2).reshape(D, E * ER)),
        "exp_out": up.reshape(K // 2, 2, P, KE * P).transpose(0, 2, 1, 3).reshape(K // 2, P, D),
        "keys_t": np.asarray(L1_ffn_lora_keys).T,
        "wq_t": np.asarray(L1_ffn_Wq).T.reshape(K, P, KEY).transpose(1, 0, 2).reshape(P, K * KEY),
    }
    ins = {name: np.ascontiguousarray(a) for name, a in ins.items()}
    nc = bacc.Bacc("TRN2", target_bir_lowering=False, num_devices=1, dynamic_dma_scratch_size=8192)
    args = {name: nc.dram_tensor(name + "_in", a.shape, mybir.dt.from_np(a.dtype), kind="ExternalInput").ap()
            for name, a in ins.items()}
    out_t = nc.dram_tensor("out_t", (K, P, B * S), F32, kind="ExternalOutput").ap()
    build(nc, out_t=out_t, **args)
    r = run_bass_kernel_spmd(nc, [{name + "_in": a for name, a in ins.items()}], core_ids=[0])
    got = np.asarray(r.results[0]["out_t"])
    return np.ascontiguousarray(got.transpose(2, 0, 1).reshape(B, S, D))
```

```python
from contextlib import ExitStack

import concourse.bass as bass
from concourse import mybir
from concourse.alu_op_type import AluOpType as ALU

F32 = mybir.dt.float32
F32R = mybir.dt.float32r
I32 = mybir.dt.int32
ACT = mybir.ActivationFunctionType
AX_X = mybir.AxisListType.X

P = 128
B, S, D = 32, 64, 1024
K = D // P
HALVES = 2
TOK = B * S // HALVES
TN = 512
TILES = TOK // TN
BT = TN // S
BH = TOK // S
PAIRS = BH // 2
RANK = 16
E, ER = 8, 64
KE = E * ER // P
NCOND = 16
SLOTS = 4
ROUNDS = PAIRS // SLOTS
MIXED_BANK = [0, 4, 6, 2]

UPGATE = 0
DOWN = UPGATE + 2 * K
LORA_A = DOWN + K
LINEAR = LORA_A + TILES
EXPERT_IN = LINEAR + K
FINAL = EXPERT_IN + KE
UNITS = FINAL + K + K // 2
USES = UNITS // 2
LOADS = USES - 1

BANK_USES = [22, 22, 21, 21, 2, 2]
FULLS = [22, 4, 21, 0, 1]
USE_UPGATE, USE_DOWN, USE_LINEAR, USE_EXPERT = 0, 8, 12, 16
USE_FINAL = [18, 18, 17, 17]
EXPERT_BANK = [0, 2, 4, 0]
EXPERT_USE = [16, 16, 1, 17]
EXPERT_FILL = [17, 17, 1, 18]
FINAL_FILL = [19, 1, 18]
KEY = 128
SCORE_SCALE = 1.0 / (S * KEY ** 0.5)
USE_XR = 0


def build(nc, x_pairs, x_t, idx, cond_t, w_upgate, b_upgate, w_down, b_down,
          w_linear, lora_a, lora_b, w_org, exp_in, exp_out, keys_t, wq_t, out_t):
    with ExitStack() as ctx:
        def sb(name, shape, dt=F32):
            return ctx.enter_context(nc.sbuf_tensor(name, shape, dt))

        def sem(name):
            return ctx.enter_context(nc.semaphore(name))

        even_hi, even_lo = sb("even_hi", [P, K, TOK], F32R), sb("even_lo", [P, K, TOK], F32R)
        odd_hi, odd_lo = sb("odd_hi", [P, K, TOK], F32R), sb("odd_lo", [P, K, TOK], F32R)
        inner = sb("inner", [P, 2, KE, TOK], F32R)
        g_hi, g_lo = inner[:, 0], inner[:, 1]
        xr = inner[:, :, 0]
        bs = inner[:, :, 1, 0:2 * TILES * P].rearrange("p h (s t m) -> p h s t m", s=2, t=TILES)
        w_hi, w_lo = sb("w_hi", [P, 2, K, P], F32R), sb("w_lo", [P, 2, K, P], F32R)
        w_raw = sb("w_raw", [P, 2, K * P])
        x_raw = sb("x_raw", [P, 2, K * P])
        gathered = sb("gathered", [P, TILES, D])
        x_slots = [x_raw[:, 0, :], x_raw[:, 1, :], gathered[:, 0, :], gathered[:, 1, :]]
        cond_sb = sb("cond_sb", [P, NCOND, S])
        mix = sb("mix", [P, PAIRS, P])
        work = sb("work", [P, 4, TN])
        idx_sb = sb("idx_sb", [1, B + BH], I32)
        b_up_sb = sb("b_up_sb", [P, 2 * K])
        b_dn_sb = sb("b_dn_sb", [P, K])
        keys_sb = sb("keys_sb", [P, E])
        mask = sb("mask", [P, BT])
        ident = sb("ident", [BH, BH])
        y_sum = sb("y_sum", [P, K, BH])
        q_sb = sb("q_sb", [P, BH])
        smax, sbias = sb("smax", [BH, 1]), sb("sbias", [BH, 1])
        ssum, sinv = sb("ssum", [BH, 1]), sb("sinv", [BH, 1])
        sexp = sb("sexp", [BH, E])
        coef_rows = sb("coef_rows", [BH, E, ER])
        coef = sb("coef", [P, KE, BH])

        banks = ctx.enter_context(nc.psum_tensor("banks", [P, 8, TN], F32))
        mixed = [banks[:, b:b + 2, :].rearrange("p a (c m) -> p (a c) m", m=P) for b in MIXED_BANK]
        router = banks[:, 7, :]

        small_loaded = sem("small_loaded")
        idx_loaded = sem("idx_loaded")
        mix_zeroed = sem("mix_zeroed")
        consts_made = sem("consts_made")
        raw_loaded = [sem(f"raw_loaded{s}") for s in range(2)]
        x_loaded = [sem(f"x_loaded{c}") for c in range(4)]
        a_gathered = [sem(f"a_gathered{s}") for s in range(2)]
        w_hi_done = [sem(f"w_hi_done{s}") for s in range(2)]
        w_ready = [sem(f"w_ready{s}") for s in range(2)]
        unit_done = [sem(f"unit_done{s}") for s in range(2)]
        cond_loaded = sem("cond_loaded")
        mix_made = [sem("mix_made0"), sem("mix_made1_even"), sem("mix_made1_odd")]
        b_gathered = sem("b_gathered")
        b_hi_done = sem("b_hi_done")
        b_split = sem("b_split")
        wq_loaded = sem("wq_loaded")
        mixed_full = [sem(f"mixed_full{c}") for c in range(SLOTS)]
        h_hi_done = sem("h_hi_done")
        h_ready = [sem(f"h_ready{c}") for c in range(SLOTS)]
        bank_full = [sem(f"bank_full{b}") for b in range(5)]
        bank_free = [sem(f"bank_free{b}") for b in range(6)]
        gated_hi_done = [sem(f"gated_hi_done{t}") for t in range(TILES)]
        gated_ready = [sem(f"gated_ready{t}") for t in range(TILES)]
        xres_loaded = [sem(f"xres_loaded{t}") for t in range(TILES)]
        x1_hi_done = [sem(f"x1_hi_done{t}") for t in range(TILES)]
        x1_ready = [sem(f"x1_ready{t}") for t in range(TILES)]
        xr_hi_done = [sem(f"xr_hi_done{t}") for t in range(TILES)]
        xr_ready = [sem(f"xr_ready{t}") for t in range(TILES)]
        y_hi_done = [sem(f"y_hi_done{t}") for t in range(TILES)]
        g_hi_done = [sem(f"g_hi_done{t}") for t in range(TILES)]
        g_ready = [sem(f"g_ready{t}") for t in range(TILES)]
        q_full = sem("q_full")
        q_copied = sem("q_copied")
        scores_full = sem("scores_full")
        max_done = sem("max_done")
        bias_done = sem("bias_done")
        exp_done = sem("exp_done")
        inv_done = sem("inv_done")
        rows_done = sem("rows_done")
        coef_full = sem("coef_full")
        coef_ready = sem("coef_ready")
        x1_summed = sem("x1_summed")
        stored = [sem(f"stored{b}") for b in range(4)]

        passed = sem("passed")

        FIRST = 1

        def start_from_one(eng, semaphores):
            for semaphore in semaphores:
                eng.sem_inc(semaphore, FIRST)

        def wait_alone(eng, semaphore, count):
            eng.wait_ge(semaphore, count)
            eng.sem_inc(passed, 1)

        def use(h, u):
            return h * USES + u

        def load_count(h, pair, gather_seen):
            return h * LOADS + pair + 1 - gather_seen

        def tok(t):
            return slice(t * TN, (t + 1) * TN)

        def wait_group(eng, h, b, s, fills, pair):
            if b % 2 == 0:
                eng.wait_ge(bank_full[b], h * FULLS[b] + fills)
            else:
                eng.wait_ge(unit_done[s], FIRST + use(h, pair) + 1)

        def in_order(unit):
            return unit.rearrange("p k m -> p (k m)")

        def as_gathered(raw):
            return raw.rearrange("p (b k r) -> p b k r", k=K, r=RANK)

        def of_gather(unit):
            return unit.rearrange("p k (b r) -> p b k r", r=RANK)

        def chunk(buf, k, t):
            return buf[:, bass.ds(k, 1), tok(t)].rearrange("p a n -> p (a n)")

        def make_mixing(eng, copy, half, blocks):
            with eng.Fori(0, PAIRS // 2) as i:
                for parity, j in blocks:
                    rows = slice(j * S, (j + 1) * S)
                    v = eng.value_load(idx_sb[0:1, bass.ds(half * BH + i * 4 + parity * 2 + j, 1)],
                                       min_val=0, max_val=NCOND - 1)
                    eng.wait_ge(cond_loaded, 32)
                    copy(mix[rows, bass.ds(i * 2 + parity, 1), rows].rearrange("p a m -> p (a m)"),
                         cond_sb[rows, bass.ds(v, 1), :].rearrange("p a m -> p (a m)")).then_inc(
                        mix_made[j * (1 + parity)], 1)

        def sync_engine(sp):
            sp.dma_start(idx_sb[:, :], idx).then_inc(idx_loaded, 16)

            def load(h, pair, s, src, seen):
                sp.wait_ge(w_ready[s], FIRST + use(h, pair))
                sp.dma_start(w_raw[:, s, :], src).then_inc(raw_loaded[s], 16)

            def half(h):
                def load_x(q, c):
                    sp.wait_ge(mixed_full[c], FIRST + h * ROUNDS + q)
                    sp.dma_start(x_slots[c], x_pairs[h * PAIRS + q * SLOTS + c]).then_inc(x_loaded[c], 16)

                load_x(0, 0)
                load_x(0, 1)
                load(h, UPGATE // 2, 0, w_upgate[0], 0)
                wait_alone(sp, q_full, FIRST + h)
                wait_alone(sp, b_split, FIRST + h * K)
                load_x(0, 2)
                load_x(0, 3)
                for q in range(1, ROUNDS):
                    for c in range(SLOTS):
                        load_x(q, c)
                load(h, UPGATE // 2, 1, w_upgate[1], 0)
                with sp.Fori(1, K) as m:
                    for s in range(2):
                        load(h, UPGATE // 2 + m, s, w_upgate[m * 2 + s], 0)
                with sp.Fori(0, K // 2) as i:
                    for s in range(2):
                        load(h, DOWN // 2 + i, s, w_down[i * 2 + s], 0)
                sp.wait_ge(idx_loaded, 16)
                for t in range(TILES):
                    wait_alone(sp, w_ready[t], FIRST + use(h, LORA_A // 2))
                    with sp.Fori(0, BT) as b:
                        v = sp.value_load(idx_sb[0:1, bass.ds(h * BH + t * BT + b, 1)],
                                          min_val=0, max_val=NCOND - 1)
                        sp.dma_start(w_raw[:, t, bass.ds(b * P, P)], lora_a[v]).then_inc(a_gathered[t], 16)
                with sp.Fori(0, K // 2) as i:
                    for s in range(2):
                        load(h, LINEAR // 2 + i, s, w_linear[i * 2 + s], 1)
                for s in range(2):
                    load(h, EXPERT_IN // 2, s, exp_in[s], 1)
                sp.wait_ge(b_split, FIRST + (h + 1) * K)
                sp.dma_start(gathered[:, 0, :], wq_t).then_inc(wq_loaded, 16)
                for s in range(2):
                    load(h, EXPERT_IN // 2 + 1, s, exp_in[2 + s], 1)
                with sp.Fori(0, 2) as q:
                    srcs = [w_org[q * 4], w_org[q * 4 + 1], exp_out[q * 2],
                            w_org[q * 4 + 2], w_org[q * 4 + 3], exp_out[q * 2 + 1]]
                    for j, src in enumerate(srcs):
                        load(h, FINAL // 2 + q * 3 + j // 2, j % 2, src, 1)

            with sp.Fori(0, HALVES) as h:
                half(h)
            load(HALVES, 0, 0, w_upgate[0], 0)

        def pool_engine(pool):
            pool.wait_ge(idx_loaded, 16)
            make_mixing(pool, pool.tensor_copy, 0, [(0, 0), (1, 0)])
            for dst, src in ((b_up_sb, b_upgate), (b_dn_sb, b_down), (keys_sb, keys_t)):
                pool.dma_start(dst[:, :], src).then_inc(small_loaded, 16)
            pool.memset(mask[:, :], 1.0).then_inc(consts_made, 1)
            pool.memset(ident[:, :], 0.0).then_inc(consts_made, 1)
            pool.wait_ge(consts_made, 2)
            pool.affine_select(out=mask[:, :], in_=mask[:, :], compare_op=ALU.is_ge, fill=0.0, base=0,
                               pattern=[[-RANK, BT]], channel_multiplier=1).then_inc(consts_made, 1)
            pool.wait_ge(consts_made, 3)
            pool.affine_select(out=mask[:, :], in_=mask[:, :], compare_op=ALU.is_ge, fill=0.0, base=RANK - 1,
                               pattern=[[RANK, BT]], channel_multiplier=-1).then_inc(consts_made, 1)
            pool.affine_select(out=ident[:, :], in_=ident[:, :], compare_op=ALU.not_equal, fill=1.0, base=0,
                               pattern=[[-1, BH]], channel_multiplier=1).then_inc(consts_made, 1)

            def load_xres(h, n, t):
                pool.dma_start(work[:, t, :], x_t[n, :, bass.ds(h * TOK + t * TN, TN)]).then_inc(
                    xres_loaded[t], 16)

            def half(h):
                wait_alone(pool, mixed_full[SLOTS - 1], FIRST + (h + 1) * ROUNDS)
                for b in range(BH):
                    v = pool.value_load(idx_sb[0:1, bass.ds(h * BH + b, 1)], min_val=0, max_val=NCOND - 1)
                    r = (b % BT) * RANK
                    pool.dma_start(gathered[r:r + RANK, b // BT, :], lora_b[v]).then_inc(b_gathered, 16)
                make_mixing(pool, pool.tensor_copy, h + 1, [(0, 0), (1, 0)])
                wait_alone(pool, mix_made[0], (h + 2) * PAIRS)
                make_mixing(pool, pool.tensor_copy, h + 1, [(0, 1), (1, 1)])
                wait_alone(pool, mix_made[2], (h + 2) * (PAIRS // 2))
                for t in range(TILES):
                    pool.wait_ge(bank_free[2 + t], FIRST + h * BANK_USES[2] + USE_DOWN)
                    load_xres(h, 0, t)
                with pool.Fori(0, K // 2 - 1) as i:
                    for j in range(2):
                        for t in range(TILES):
                            b = 2 * j + t
                            pool.wait_ge(bank_free[b], FIRST + h * BANK_USES[b] + USE_DOWN + i + 1)
                            load_xres(h, i * 2 + j + 1, t)
                for t in range(TILES):
                    pool.wait_ge(bank_free[t], FIRST + h * BANK_USES[t] + USE_DOWN + K // 2)
                    load_xres(h, K - 1, t)

            pool.wait_ge(consts_made, 5)
            with pool.Fori(0, HALVES) as h:
                half(h)

        def tensor_engine(pe):
            start_from_one(pe, unit_done + mixed_full + [q_full])

            def product(out, stat_hi, stat_lo, mov_hi, mov_lo, start, stop):
                pe.matmul(out, stat_hi, mov_hi, start=start, stop=False)
                pe.matmul(out, stat_hi, mov_lo, start=False, stop=False)
                return pe.matmul(out, stat_lo, mov_hi, start=False, stop=stop)

            def chunks(b, s, hi, lo, t, count=K, tile0=0, start=True, stop=True, last_wait=None):
                for k in range(count):
                    if k == count - 1 and last_wait is not None:
                        last_wait()
                    last = product(banks[:, b, :], w_hi[:, s, tile0 + k, :], w_lo[:, s, tile0 + k, :],
                                   hi[:, k, tok(t)], lo[:, k, tok(t)],
                                   start and k == 0, stop and k == count - 1)
                return last

            def half(h):
                with pe.Fori(0, ROUNDS) as q:
                    for c in range(SLOTS):
                        pe.wait_ge(mix_made[0], h * PAIRS + q * SLOTS + c + 1)
                        pe.wait_ge(mix_made[1 + c % 2], h * (PAIRS // 2) + q * (SLOTS // 2) + c // 2 + 1)
                        pe.wait_ge(x_loaded[c], (h * ROUNDS + q + 1) * 16)
                        pe.wait_ge(h_ready[c], FIRST + h * ROUNDS + q)
                        if MIXED_BANK[c] < 4:
                            for b in (MIXED_BANK[c], MIXED_BANK[c] + 1):
                                pe.wait_ge(bank_free[b], FIRST + h * BANK_USES[b])
                        matrix = mix[:, bass.ds(q * SLOTS + c, 1), :].rearrange("p a m -> p (a m)")
                        for k in range(K):
                            last = pe.matmul(mixed[c][:, k, :], x_slots[c][:, k * P:(k + 1) * P], matrix,
                                             start=True, stop=True)
                        last.then_inc(mixed_full[c], 1)
                for c in range(SLOTS):
                    count = ROUNDS if MIXED_BANK[c] == 0 else ROUNDS // TILES
                    wait_alone(pe, h_ready[c], FIRST + h * ROUNDS + count)
                with pe.Fori(0, K) as m:
                    for s in range(2):
                        pe.wait_ge(w_ready[s], FIRST + use(h, UPGATE // 2 + m) + 1)
                        for t in range(TILES):
                            b = 2 * s + t
                            if t == 1:
                                for c in range(SLOTS):
                                    pe.wait_ge(h_ready[c], FIRST + (h + 1) * ROUNDS)
                            pe.wait_ge(bank_free[b], FIRST + h * BANK_USES[b] + USE_UPGATE + m)
                            chunks(b, s, even_hi, even_lo, t).then_inc(unit_done[s] if t else bank_full[b], 1)
                with pe.Fori(0, K // 2) as i:
                    for s in range(2):
                        pe.wait_ge(w_ready[s], FIRST + use(h, DOWN // 2 + i) + 1)
                        for t in range(TILES):
                            b = 2 * s + t
                            pe.wait_ge(bank_free[b], FIRST + h * BANK_USES[b] + USE_DOWN + i)
                            pe.wait_ge(gated_ready[t], h * K + K - 1)
                            chunks(b, s, odd_hi, odd_lo, t,
                                   last_wait=lambda: pe.wait_ge(gated_ready[t], h * K + K),
                                   ).then_inc(unit_done[s] if t else bank_full[b], 1)
                for t in range(TILES):
                    pe.wait_ge(w_ready[t], FIRST + use(h, LORA_A // 2) + 1)
                    pe.wait_ge(x1_ready[t], h * K + K - 1)
                    chunks(4 + t, t, even_hi, even_lo, t,
                           last_wait=lambda: pe.wait_ge(x1_ready[t], h * K + K),
                           ).then_inc(unit_done[t], 1)
                with pe.Fori(0, K // 2) as i:
                    for s in range(2):
                        pe.wait_ge(w_ready[s], FIRST + use(h, LINEAR // 2 + i) + 1)
                        for t in range(TILES):
                            b = 2 * s + t
                            pe.wait_ge(bank_free[b], FIRST + h * BANK_USES[b] + USE_LINEAR + i)
                            chunks(b, s, even_hi, even_lo, t, stop=False)
                            pe.wait_ge(xr_ready[t], h + 1)
                            product(banks[:, b, :], bs[:, 0, s, t], bs[:, 1, s, t], xr[:, 0, tok(t)],
                                    xr[:, 1, tok(t)], False, True).then_inc(unit_done[s] if t else bank_full[b], 1)
                for e in range(KE):
                    s = e % 2
                    pe.wait_ge(w_ready[s], FIRST + use(h, EXPERT_IN // 2 + e // 2) + 1)
                    for t in range(TILES):
                        b = EXPERT_BANK[e] + t
                        if e in (0, 1, 3):
                            pe.wait_ge(bank_free[b], FIRST + h * BANK_USES[b] + EXPERT_USE[e])
                        pe.wait_ge(bank_free[t], FIRST + h * BANK_USES[t] + USE_EXPERT)
                        chunks(b, s, odd_hi, odd_lo, t,
                               last_wait=lambda: pe.wait_ge(bank_free[2 + t], FIRST + h * BANK_USES[2] + USE_EXPERT),
                               ).then_inc(unit_done[s] if t else bank_full[b], 1)
                        if e == 1 and t == 0:
                            pe.wait_ge(q_copied, h + 1)
                            pe.wait_ge(small_loaded, 48)
                            pe.matmul(router[0:BH, 32:32 + E], q_sb[:, :], keys_sb[:, :],
                                      start=True, stop=True).then_inc(scores_full, 1)
                    if e == 0:
                        pe.wait_ge(wq_loaded, (h + 1) * 16)
                        for k in range(K):
                            last = pe.matmul(router[:, 0:BH], gathered[:, 0, k * P:(k + 1) * P],
                                             y_sum[:, k, :], start=(k == 0), stop=(k == K - 1))
                        last.then_inc(q_full, 1)
                    if e == 1:
                        pe.wait_ge(rows_done, h + 1)
                        pe.wait_ge(consts_made, 5)
                        for k in range(KE):
                            rows = coef_rows[:, 2 * k:2 * k + 2, :].rearrange("b e r -> b (e r)")
                            last = pe.matmul(router[:, 64 + k * BH:64 + (k + 1) * BH], rows, ident[:, :],
                                             start=True, stop=True)
                        last.then_inc(coef_full, 1)
                with pe.Fori(0, 2) as q:
                    for j in range(6):
                        s = j % 2
                        pe.wait_ge(w_ready[s], FIRST + use(h, FINAL // 2 + q * 3 + j // 2) + 1)
                        if j % 3 < 2:
                            for t in range(TILES):
                                b = 2 * (j % 3) + t
                                pe.wait_ge(bank_free[b], FIRST + h * BANK_USES[b] + USE_FINAL[b] + q * 2 + j // 3)
                                last = chunks(b, s, odd_hi, odd_lo, t, stop=False)
                            if t == TILES - 1:
                                last.then_inc(unit_done[s], 1)
                        else:
                            for b in range(4):
                                pe.wait_ge(g_ready[b % 2], (h + 1) * KE)
                                last = chunks(b, s, g_hi, g_lo, b % 2, count=KE, tile0=KE * (b // 2),
                                              start=False)
                                last.then_inc(unit_done[s] if b == 3 else bank_full[b], 1)

            pe.wait_ge(mix_zeroed, 2)
            with pe.Fori(0, HALVES) as h:
                half(h)

        def scalar_engine(act):
            def split(h, pair, s, seen=0, gather=False):
                raw = w_raw[:, s, :]
                if gather:
                    act.wait_ge(a_gathered[s], (h + 1) * BT * 16)
                else:
                    act.wait_ge(raw_loaded[s], load_count(h, pair, seen) * 16)
                act.wait_ge(unit_done[s], FIRST + use(h, pair))
                hi = w_hi[:, s, :, :]
                act.copy(of_gather(hi) if gather else in_order(hi), as_gathered(raw) if gather else raw
                         ).then_inc(w_hi_done[s], 1)

            def half(h):
                act.wait_ge(x1_summed, FIRST + h * 2 * K)
                with act.Fori(0, ROUNDS) as q:
                    for c in range(SLOTS):
                        act.wait_ge(mixed_full[c], FIRST + h * ROUNDS + q + 1)
                        act.copy(even_hi[:, :, bass.ds((q * SLOTS + c) * P, P)], mixed[c]).then_inc(h_hi_done, 1)
                for t in range(TILES):
                    act.wait_ge(stored[t], FIRST + h * (K // 2) * 16)
                act.wait_ge(small_loaded, 48)
                with act.Fori(0, K) as m:
                    split(h, UPGATE // 2 + m, 1)
                    for t in range(TILES):
                        wait_group(act, h, t, 0, USE_UPGATE + m + 1, UPGATE // 2 + m)
                        act.sem_inc(passed, 1)
                        act.activation(work[:, t, :], banks[:, t, :], ACT.Silu,
                                       bias=b_up_sb[:, bass.ds(m, 1)]).then_inc(bank_free[t], 1)
                    split(h, UPGATE // 2 + m + 1, 0)
                    for t in range(TILES):
                        act.wait_ge(bank_free[2 + t], FIRST + h * BANK_USES[2] + USE_UPGATE + m + 1)
                        act.copy(chunk(odd_hi, m, t),
                                 work[:, 2 + t, :]).then_inc(gated_hi_done[t], 1)

                def down(i, last):
                    for s in range(2):
                        if s == 0:
                            split(h, DOWN // 2 + i, 1)
                        else:
                            split(h, DOWN // 2 + i + 1, 0, gather=last)
                        for t in range(TILES):
                            b = 2 * s + t
                            act.wait_ge(bank_free[b], FIRST + h * BANK_USES[b] + USE_DOWN + i + 1)
                            act.copy(chunk(even_hi, i * 2 + s, t),
                                     work[:, 2 + t, :]).then_inc(x1_hi_done[t], 1)

                with act.Fori(0, K // 2 - 1) as i:
                    down(i, False)
                down(K // 2 - 1, True)

                def split_linear(pair, s, n):
                    act.wait_ge(unit_done[s], FIRST + use(h, pair))
                    act.copy(bs[:, 0, s], gathered[:, :, bass.ds(n * P, P)]).then_inc(b_hi_done, 1)
                    split(h, pair, s, seen=1)

                act.wait_ge(b_gathered, (h + 1) * BH * 16)
                split(h, LORA_A // 2, 1, gather=True)
                for t in range(TILES):
                    if t == 1:
                        split_linear(LINEAR // 2, 0, 0)
                    act.wait_ge(bank_free[4 + t], FIRST + h * BANK_USES[4] + USE_XR + 1)
                    act.copy(xr[:, 0, tok(t)], work[:, 2 + t, :]).then_inc(xr_hi_done[t], 1)

                def linear(i, last):
                    for s in range(2):
                        if s == 0:
                            split_linear(LINEAR // 2 + i, 1, i * 2 + 1)
                        elif not last:
                            split_linear(LINEAR // 2 + i + 1, 0, i * 2 + 2)
                        else:
                            split(h, EXPERT_IN // 2, 0, seen=1)
                        for t in range(TILES):
                            b = 2 * s + t
                            wait_group(act, h, b, s, USE_LINEAR + i + 1, LINEAR // 2 + i)
                            act.copy(chunk(odd_hi, i * 2 + s, t),
                                     banks[:, b, :]).then_inc(y_hi_done[t], 1)

                with act.Fori(0, K // 2 - 1) as i:
                    linear(i, False)
                linear(K // 2 - 1, True)

                split(h, EXPERT_IN // 2, 1, seen=1)
                split(h, EXPERT_IN // 2 + 1, 0, seen=1)
                act.wait_ge(bias_done, h + 1)
                act.activation(sexp[:, :], router[0:BH, 32:32 + E], ACT.Exp, bias=sbias[:, :],
                               scale=SCORE_SCALE, accum_out=ssum[:, :]).then_inc(exp_done, 1)

                def expert_hi(e):
                    for t in range(TILES):
                        b = EXPERT_BANK[e] + t
                        act.wait_ge(bank_free[b], FIRST + h * BANK_USES[b] + EXPERT_USE[e] + 1)
                        act.copy(g_hi[:, e, tok(t)], work[:, 2 + t, :]).then_inc(g_hi_done[t], 1)

                expert_hi(0)
                split(h, EXPERT_IN // 2 + 1, 1, seen=1)
                expert_hi(1)
                split(h, FINAL // 2, 0, seen=1)
                expert_hi(2)
                expert_hi(3)
                with act.Fori(0, 2) as q:
                    for j in range(1, 7):
                        split(h, FINAL // 2 + q * 3 + j // 2, j % 2, seen=1)
                        if j % 3 == 0:
                            i = q * 2 + j // 3 - 1
                            for b in range(4):
                                act.wait_ge(bank_free[b], FIRST + h * BANK_USES[b] + USE_FINAL[b] + i + 1)
                                act.dma_start(out_t[i * 2 + b // 2, :, bass.ds(h * TOK + (b % 2) * TN, TN)],
                                              work[:, b, :]).then_inc(stored[b], 16)

            for j in range(2):
                act.dma_start(cond_sb[j * S:(j + 1) * S, :, :], cond_t).then_inc(cond_loaded, 16)
            act.wait_ge(idx_loaded, 16)
            make_mixing(act, act.copy, 0, [(1, 1)])
            start_from_one(act, stored)
            split(0, 0, 0)
            with act.Fori(0, HALVES) as h:
                half(h)
            for b in range(4):
                act.wait_ge(stored[b], FIRST + HALVES * (K // 2) * 16)

        def vector_engine(dve):
            start_from_one(dve, w_ready + [b_split, x1_summed] + h_ready + bank_free)

            def lo(out, value, hi):
                return dve.tensor_tensor(out, value, hi.bitcast(F32), ALU.subtract)

            def split(h, pair, s, gather=False):
                dve.wait_ge(w_hi_done[s], use(h, pair) + 1)
                raw = w_raw[:, s, :]
                view, raw = (of_gather, as_gathered(raw)) if gather else (in_order, raw)
                lo(view(w_lo[:, s, :, :]), raw, view(w_hi[:, s, :, :])).then_inc(w_ready[s], 1)

            dve.memset(mix[0:S, :, S:P], 0.0).then_inc(mix_zeroed, 1)
            dve.memset(mix[S:P, :, 0:S], 0.0).then_inc(mix_zeroed, 1)
            dve.wait_ge(idx_loaded, 16)
            make_mixing(dve, dve.tensor_copy, 0, [(0, 1)])

            def half(h):
                with dve.Fori(0, ROUNDS) as q:
                    for c in range(SLOTS):
                        dve.wait_ge(h_hi_done, h * PAIRS + q * SLOTS + c + 1)
                        cols = bass.ds((q * SLOTS + c) * P, P)
                        lo(even_lo[:, :, cols], mixed[c], even_hi[:, :, cols]).then_inc(h_ready[c], 1)
                for t in range(TILES):
                    wait_alone(dve, stored[2 + t], FIRST + h * (K // 2) * 16)
                dve.wait_ge(small_loaded, 48)
                with dve.Fori(0, K) as m:
                    split(h, UPGATE // 2 + m, 1)
                    split(h, UPGATE // 2 + m + 1, 0)
                    for t in range(TILES):
                        dve.wait_ge(bank_free[t], FIRST + h * BANK_USES[t] + USE_UPGATE + m + 1)
                        wait_group(dve, h, 2 + t, 1, USE_UPGATE + m + 1, UPGATE // 2 + m)
                        dve.scalar_tensor_tensor(out=work[:, 2 + t, :], in0=banks[:, 2 + t, :],
                                                 scalar=b_up_sb[:, bass.ds(m + K, 1)], in1=work[:, t, :],
                                                 op0=ALU.add, op1=ALU.mult).then_inc(bank_free[2 + t], 1)
                        dve.wait_ge(gated_hi_done[t], h * K + m + 1)
                        lo(chunk(odd_lo, m, t), work[:, 2 + t, :], chunk(odd_hi, m, t)).then_inc(
                            gated_ready[t], 1)
                def down(i, last):
                    for s in range(2):
                        split(h, DOWN // 2 + i + s, 1 - s, gather=last and s == 1)
                        for t in range(TILES):
                            b, n = 2 * s + t, i * 2 + s
                            wait_group(dve, h, b, s, USE_DOWN + i + 1, DOWN // 2 + i)
                            dve.wait_ge(xres_loaded[t], (h * K + n + 1) * 16)
                            dve.scalar_tensor_tensor(out=work[:, 2 + t, :], in0=banks[:, b, :],
                                                     scalar=b_dn_sb[:, bass.ds(n, 1)], in1=work[:, t, :],
                                                     op0=ALU.add, op1=ALU.add).then_inc(bank_free[b], 1)
                            dve.wait_ge(x1_hi_done[t], h * K + n + 1)
                            lo(chunk(even_lo, n, t), work[:, 2 + t, :], chunk(even_hi, n, t)).then_inc(
                                x1_ready[t], 1)

                with dve.Fori(0, K // 2 - 1) as i:
                    down(i, False)
                down(K // 2 - 1, True)

                def split_linear(pair, s, n):
                    dve.wait_ge(b_hi_done, h * K + n + 1)
                    lo(bs[:, 1, s], gathered[:, :, bass.ds(n * P, P)], bs[:, 0, s]).then_inc(b_split, 1)
                    split(h, pair, s)

                split(h, LORA_A // 2, 1, gather=True)
                dve.wait_ge(consts_made, 5)
                for t in range(TILES):
                    if t == 1:
                        split_linear(LINEAR // 2, 0, 0)
                    dve.wait_ge(unit_done[t], FIRST + use(h, LORA_A // 2) + 1)
                    dve.tensor_tensor(work[:, 2 + t, :].rearrange("p (b n) -> p b n", n=S),
                                      banks[:, 4 + t, :].rearrange("p (b n) -> p b n", n=S),
                                      mask[:, :].unsqueeze(2).to_broadcast([P, BT, S]),
                                      ALU.mult).then_inc(bank_free[4 + t], 1)
                    dve.wait_ge(xr_hi_done[t], h + 1)
                    lo(xr[:, 1, tok(t)], work[:, 2 + t, :], xr[:, 0, tok(t)]).then_inc(xr_ready[t], 1)

                def linear(i, last):
                    for s in range(2):
                        if s == 0:
                            split_linear(LINEAR // 2 + i, 1, i * 2 + 1)
                        elif not last:
                            split_linear(LINEAR // 2 + i + 1, 0, i * 2 + 2)
                        else:
                            split(h, EXPERT_IN // 2, 0)
                        for t in range(TILES):
                            b, n = 2 * s + t, i * 2 + s
                            dve.wait_ge(y_hi_done[t], h * K + n + 1)
                            dve.tensor_reduce(
                                y_sum[:, bass.ds(n, 1), t * BT:(t + 1) * BT].rearrange("p a b -> p (a b)"),
                                banks[:, b, :].rearrange("p (b n) -> p b n", n=S), AX_X, ALU.add)
                            lo(chunk(odd_lo, n, t), banks[:, b, :], chunk(odd_hi, n, t)).then_inc(
                                bank_free[b], 1)

                with dve.Fori(0, K // 2 - 1) as i:
                    linear(i, False)
                linear(K // 2 - 1, True)

                split(h, EXPERT_IN // 2, 1)
                dve.wait_ge(q_full, FIRST + h + 1)
                dve.tensor_copy(q_sb[:, :], router[:, 0:BH]).then_inc(q_copied, 1)
                split(h, EXPERT_IN // 2 + 1, 0)
                dve.wait_ge(scores_full, h + 1)
                dve.reduce_max(smax[:, :], router[0:BH, 32:32 + E], AX_X).then_inc(max_done, 1)
                dve.wait_ge(max_done, h + 1)
                dve.tensor_scalar(sbias[:, :], smax[:, :], -SCORE_SCALE, None, ALU.mult).then_inc(bias_done, 1)
                dve.wait_ge(exp_done, h + 1)
                dve.reciprocal(sinv[:, :], ssum[:, :]).then_inc(inv_done, 1)
                dve.wait_ge(inv_done, h + 1)
                dve.tensor_scalar(coef_rows[:, :, :], sexp[:, :].unsqueeze(2).to_broadcast([BH, E, ER]),
                                  sinv[:, :], None, ALU.mult).then_inc(rows_done, 1)
                dve.wait_ge(coef_full, h + 1)
                dve.tensor_copy(coef[:, :, :].rearrange("p k b -> p (k b)"),
                                router[:, 64:64 + KE * BH]).then_inc(coef_ready, 1)
                dve.wait_ge(coef_ready, h + 1)

                def expert(e):
                    for t in range(TILES):
                        b = EXPERT_BANK[e] + t
                        wait_group(dve, h, b, e % 2, EXPERT_FILL[e], EXPERT_IN // 2 + e // 2)
                        dve.tensor_tensor(work[:, 2 + t, :].rearrange("p (b n) -> p b n", n=S),
                                          banks[:, b, :].rearrange("p (b n) -> p b n", n=S),
                                          coef[:, e, t * BT:(t + 1) * BT].unsqueeze(2).to_broadcast([P, BT, S]),
                                          ALU.mult).then_inc(bank_free[b], 1)
                        dve.wait_ge(g_hi_done[t], h * KE + e + 1)
                        lo(g_lo[:, e, tok(t)], work[:, 2 + t, :], g_hi[:, e, tok(t)]).then_inc(g_ready[t], 1)

                expert(0)
                split(h, EXPERT_IN // 2 + 1, 1)
                expert(1)
                split(h, FINAL // 2, 0)
                expert(2)
                expert(3)
                for t in range(TILES):
                    wait_alone(dve, g_ready[t], (h + 1) * KE)
                with dve.Fori(0, 2) as q:
                    for j in range(6):
                        split(h, FINAL // 2 + q * 3 + (j + 1) // 2, (j + 1) % 2)
                        i = q * 2 + j // 3
                        if j % 3 == 0:
                            for b in range(4):
                                n, t = i * 2 + b // 2, b % 2
                                dve.wait_ge(stored[b], FIRST + (h * (K // 2) + i) * 16)
                                dve.tensor_tensor(work[:, b, :], chunk(even_hi, n, t).bitcast(F32),
                                                  chunk(even_lo, n, t).bitcast(F32), ALU.add).then_inc(x1_summed, 1)
                        if j % 3 < 2:
                            continue
                        for b in range(4):
                            if b < 3:
                                dve.wait_ge(bank_full[b], h * FULLS[b] + FINAL_FILL[b] + i)
                            else:
                                dve.wait_ge(unit_done[j % 2], FIRST + use(h, FINAL // 2 + q * 3 + j // 2) + 1)
                            dve.wait_ge(x1_summed, FIRST + h * 2 * K + i * 4 + b + 1)
                            dve.tensor_tensor(work[:, b, :], banks[:, b, :], work[:, b, :],
                                              ALU.add).then_inc(bank_free[b], 1)

            split(0, 0, 0)
            with dve.Fori(0, HALVES) as h:
                half(h)

        with nc.Block() as block:
            @block.sync
            def _(sp):
                sync_engine(sp)

            @block.gpsimd
            def _(pool):
                pool_engine(pool)

            @block.tensor
            def _(pe):
                tensor_engine(pe)

            @block.scalar
            def _(act):
                scalar_engine(act)

            @block.vector
            def _(dve):
                vector_engine(dve)


def kernel(x, itok_B_0_15, L0_cond_weights, L0_ffn_w12, L0_ffn_b12, L0_ffn_w3, L0_ffn_b3,
           L1_cond_W, L1_cond_lora_A, L1_cond_lora_B, L1_ffn_W_org, L1_ffn_lora_down,
           L1_ffn_lora_up, L1_ffn_lora_keys, L1_ffn_Wq):
    import numpy as np
    import concourse.bacc as bacc
    from concourse.bass_utils import run_bass_kernel_spmd

    def units(w):
        w = np.asarray(w)
        n = w.shape[1] // P
        return w.reshape(-1, P, n, P).transpose(2, 1, 0, 3).reshape(n, P, -1)

    x, itok = np.asarray(x), np.asarray(itok_B_0_15)
    w12 = np.asarray(L0_ffn_w12)
    upgate = units(w12.T)
    upgate = upgate.reshape(2, K, P, D).transpose(1, 0, 2, 3).reshape(2 * K, P, D)
    b12 = np.asarray(L0_ffn_b12)
    up = units(np.asarray(L1_ffn_lora_up).reshape(E * ER, D))
    lora_a = np.asarray(L1_cond_lora_A).reshape(NCOND, K, P, RANK).transpose(0, 2, 1, 3)
    ins = {
        "x_pairs": x.reshape(B // 2, P, D),
        "x_t": x.reshape(B * S, K, P).transpose(1, 2, 0),
        "idx": np.concatenate([itok, itok[:BH]]).reshape(1, B + BH),
        "cond_t": np.asarray(L0_cond_weights).transpose(1, 0, 2),
        "w_upgate": upgate,
        "b_upgate": b12.reshape(2 * K, P).T,
        "w_down": units(np.asarray(L0_ffn_w3).T),
        "b_down": np.asarray(L0_ffn_b3).reshape(K, P).T,
        "w_linear": units(L1_cond_W),
        "lora_a": lora_a.reshape(NCOND, P, K * RANK),
        "lora_b": np.asarray(L1_cond_lora_B),
        "w_org": units(np.asarray(L1_ffn_W_org).T),
        "exp_in": units(np.asarray(L1_ffn_lora_down).transpose(1, 0, 2).reshape(D, E * ER)),
        "exp_out": up.reshape(K // 2, 2, P, KE * P).transpose(0, 2, 1, 3).reshape(K // 2, P, D),
        "keys_t": np.asarray(L1_ffn_lora_keys).T,
        "wq_t": np.asarray(L1_ffn_Wq).T.reshape(K, P, KEY).transpose(1, 0, 2).reshape(P, K * KEY),
    }
    ins = {name: np.ascontiguousarray(a) for name, a in ins.items()}
    nc = bacc.Bacc("TRN2", target_bir_lowering=False, num_devices=1, dynamic_dma_scratch_size=4096)
    args = {name: nc.dram_tensor(name + "_in", a.shape, mybir.dt.from_np(a.dtype), kind="ExternalInput").ap()
            for name, a in ins.items()}
    out_t = nc.dram_tensor("out_t", (K, P, B * S), F32, kind="ExternalOutput").ap()
    build(nc, out_t=out_t, **args)
    r = run_bass_kernel_spmd(nc, [{name + "_in": a for name, a in ins.items()}], core_ids=[0])
    got = np.asarray(r.results[0]["out_t"])
    return np.ascontiguousarray(got.transpose(2, 0, 1).reshape(B, S, D))
```
